# Optimizing a Trainium2 kernel written in Bass

```python
import numpy as np
import jax
import jax.numpy as jnp

def _softmax(x, axis=-1):
    return jax.nn.softmax(x, axis=axis)

def _gelu(x):
    return jax.nn.gelu(x, approximate=True)

def _silu(x):
    return jax.nn.silu(x)

def _sigmoid(x):
    return jax.nn.sigmoid(x)

def _layernorm(x, axis=-1, eps=1e-05):
    m = jnp.mean(x, axis=axis, keepdims=True)
    v = jnp.var(x, axis=axis, keepdims=True)
    return (x - m) / jnp.sqrt(v + eps)

def _scatter_add(tgt, idx, src, axis=0):
    return tgt.at[idx].add(src)

def _segment_sum(src, seg, n):
    return jax.ops.segment_sum(src, seg, n)
kernel_name = 'mk_lm_tower_d1_tok_ids1024_r4_f4419e'

def setup_inputs(seed: int=0):
    np.random.seed(seed)
    _w = jnp.asarray

    def _rec_inputs():
        import jax
        import jax.numpy as jnp
        _rk = jax.random.key(seed)
        x = jax.random.randint(jax.random.fold_in(_rk, 1), (64, 128), 0, 31993, jnp.int32)
        return x
    x = _rec_inputs()

    def _L0_tok_setup():
        import jax, jax.numpy as jnp
        import numpy as np
        NUM_HEADS = 16
        EMBED = 256
        HEAD_DIM = EMBED // NUM_HEADS
        VOCAB = 8000
        BATCH, SEQ = (4, 512)
        key = jax.random.key(seed)
        ks = jax.random.split(key, 10)
        s = 0.02
        return {'inp': jax.random.randint(ks[0], (BATCH, SEQ), 0, VOCAB, dtype=jnp.int64 if jax.config.jax_enable_x64 else jnp.int32), 'emb': jax.random.normal(ks[1], (VOCAB, EMBED), jnp.float32) * s, 'Wq': jax.random.normal(ks[2], (EMBED, EMBED), jnp.float32) * s, 'bq': jnp.zeros((EMBED,), jnp.float32), 'Wk': jax.random.normal(ks[3], (EMBED, EMBED), jnp.float32) * s, 'bk': jnp.zeros((EMBED,), jnp.float32), 'Wv': jax.random.normal(ks[4], (EMBED, EMBED), jnp.float32) * s, 'bv': jnp.zeros((EMBED,), jnp.float32), 'Wo': jax.random.normal(ks[5], (EMBED, EMBED), jnp.float32) * s, 'bo': jnp.zeros((EMBED,), jnp.float32)}
    _L0_tok_all = _L0_tok_setup()
    _L0_tok_in = {k: v for k, v in _L0_tok_all.items() if k in ('emb', 'Wq', 'bq', 'Wk', 'bk', 'Wv', 'bv', 'Wo', 'bo')}
    del _L0_tok_all

    def _L0_attn_setup():
        import jax, jax.numpy as jnp
        import numpy as np
        import math
        B_SZ, L, D, S = (4, 1024, 256, 64)

        def _blelloch_exclusive_scan(a, b):

            def combine(p, q):
                pa, pb = p
                qa, qb = q
                return (pa * qa, pa * qb + pb)
            _, b_inc = jax.lax.associative_scan(combine, (a, b), axis=1)
            return jnp.concatenate([jnp.zeros_like(b_inc[:, :1]), b_inc[:, :-1]], axis=1)
        key = jax.random.key(seed)
        k0, k1, k2, k3 = jax.random.split(key, 4)
        x = jax.random.normal(k0, (B_SZ, L, D), dtype=jnp.float32)
        B_w = jax.random.normal(k1, (S, D), dtype=jnp.float32) * (1.0 / math.sqrt(D))
        C_w = jax.random.normal(k2, (D, S), dtype=jnp.float32) * (1.0 / math.sqrt(S))
        gate_w = jax.random.normal(k3, (D, D), dtype=jnp.float32) * (1.0 / math.sqrt(D))
        gate_b = jnp.zeros((D,), dtype=jnp.float32)
        log_decay = jnp.full((D,), math.log(0.9), dtype=jnp.float32)
        return {'x': x, 'B_w': B_w, 'C_w': C_w, 'gate_w': gate_w, 'gate_b': gate_b, 'log_decay': log_decay}
    _L0_attn_all = _L0_attn_setup()
    _L0_attn_in = {k: v for k, v in _L0_attn_all.items() if k in ('B_w', 'C_w', 'gate_w', 'gate_b', 'log_decay')}
    del _L0_attn_all

    def _L0_ffn_setup():
        import jax, jax.numpy as jnp
        import numpy as np
        key = jax.random.key(seed)
        kx, kw = jax.random.split(key)
        x = jax.random.normal(kx, (32, 1024, 256), dtype=jnp.float32)
        weight = jax.random.normal(kw, (256, 256), dtype=jnp.float32) * 0.01
        return {'x': x, 'weight': weight}
    _L0_ffn_all = _L0_ffn_setup()
    _L0_ffn_in = {k: v for k, v in _L0_ffn_all.items() if k in ('weight',)}
    del _L0_ffn_all
    return {'x': x, 'L0_tok_emb': _L0_tok_in['emb'], 'L0_tok_Wq': _L0_tok_in['Wq'], 'L0_tok_bq': _L0_tok_in['bq'], 'L0_tok_Wk': _L0_tok_in['Wk'], 'L0_tok_bk': _L0_tok_in['bk'], 'L0_tok_Wv': _L0_tok_in['Wv'], 'L0_tok_bv': _L0_tok_in['bv'], 'L0_tok_Wo': _L0_tok_in['Wo'], 'L0_tok_bo': _L0_tok_in['bo'], 'L0_attn_B_w': _L0_attn_in['B_w'], 'L0_attn_C_w': _L0_attn_in['C_w'], 'L0_attn_gate_w': _L0_attn_in['gate_w'], 'L0_attn_gate_b': _L0_attn_in['gate_b'], 'L0_attn_log_decay': _L0_attn_in['log_decay'], 'L0_ffn_weight': _L0_ffn_in['weight']}

def reference(x, L0_tok_emb, L0_tok_Wq, L0_tok_bq, L0_tok_Wk, L0_tok_bk, L0_tok_Wv, L0_tok_bv, L0_tok_Wo, L0_tok_bo, L0_attn_B_w, L0_attn_C_w, L0_attn_gate_w, L0_attn_gate_b, L0_attn_log_decay, L0_ffn_weight):
    import jax
    import jax.numpy as jnp

    def _L0_tok_ref(inp, emb, Wq, bq, Wk, bk, Wv, bv, Wo, bo):
        import jax, jax.numpy as jnp
        import numpy as np
        NUM_HEADS = 16
        EMBED = 256
        HEAD_DIM = EMBED // NUM_HEADS
        VOCAB = 8000
        BATCH, SEQ = (4, 512)
        x = emb[inp]
        q = x @ Wq.T + bq
        k = x @ Wk.T + bk
        v = x @ Wv.T + bv

        def split(t):
            B, S, _ = t.shape
            return t.reshape(B, S, NUM_HEADS, HEAD_DIM).transpose(0, 2, 1, 3)
        q, k, v = (split(q), split(k), split(v))
        scale = 1.0 / jnp.sqrt(jnp.float32(HEAD_DIM))
        scores = jnp.einsum('bhqd,bhkd->bhqk', q, k) * scale
        attn = jax.nn.softmax(scores, axis=-1)
        ctx = jnp.einsum('bhqk,bhkd->bhqd', attn, v)
        B, H, S, hd = ctx.shape
        ctx = ctx.transpose(0, 2, 1, 3).reshape(B, S, H * hd)
        return ctx @ Wo.T + bo

    def _L0_attn_ref(x, B_w, C_w, gate_w, gate_b, log_decay):
        import jax, jax.numpy as jnp
        import numpy as np
        import math
        B_SZ, L, D, S = (4, 1024, 256, 64)

        def _blelloch_exclusive_scan(a, b):

            def combine(p, q):
                pa, pb = p
                qa, qb = q
                return (pa * qa, pa * qb + pb)
            _, b_inc = jax.lax.associative_scan(combine, (a, b), axis=1)
            return jnp.concatenate([jnp.zeros_like(b_inc[:, :1]), b_inc[:, :-1]], axis=1)
        Bu = jnp.einsum('bld,sd->bls', x, B_w)
        Bu_proj = jnp.einsum('bls,ds->bld', Bu, C_w)
        decay = jax.nn.sigmoid(log_decay)
        a = jnp.broadcast_to(decay, Bu_proj.shape)
        h = _blelloch_exclusive_scan(a, Bu_proj)
        gate = jax.nn.sigmoid(jnp.einsum('bld,ed->ble', x, gate_w) + gate_b)
        return gate * h

    def _L0_ffn_ref(x, weight):
        import jax, jax.numpy as jnp
        import numpy as np
        b_weight = jnp.sign(weight)
        return jnp.einsum('bsi,oi->bso', x, b_weight)
    h = _L0_tok_ref(x, L0_tok_emb, L0_tok_Wq, L0_tok_bq, L0_tok_Wk, L0_tok_bk, L0_tok_Wv, L0_tok_bv, L0_tok_Wo, L0_tok_bo)
    h = h + _L0_attn_ref(_layernorm(h, axis=-1), L0_attn_B_w, L0_attn_C_w, L0_attn_gate_w, L0_attn_gate_b, L0_attn_log_decay)
    h = h + _L0_ffn_ref(_layernorm(h, axis=-1), L0_ffn_weight)
    return h

_drawn_inputs = setup_inputs


def setup_inputs(seed=0):
    import zlib

    import numpy as np

    out = dict(_drawn_inputs(seed))
    spreads = {'L0_tok_bq': (0.0, 2.0),
     'L0_tok_bk': (0.0, 2.0),
     'L0_tok_bv': (0.0, 0.1),
     'L0_tok_bo': (0.0, 0.1),
     'L0_attn_gate_b': (0.0, 0.1),
     'L0_attn_log_decay': (-0.10536051541566849, 0.6)}
    factors = {'L0_tok_emb': 3.87, 'L0_tok_Wq': 64.0, 'L0_tok_Wk': 64.0, 'L0_tok_Wv': 3.364}
    for name, (base, spread) in spreads.items():
        noise = np.random.default_rng([zlib.crc32(name.encode()), seed]).standard_normal(out[name].shape)
        drawn = base * np.exp(spread * noise) if base else spread * noise
        out[name] = jnp.asarray(drawn.astype(out[name].dtype))
    for name, factor in factors.items():
        out[name] = (out[name] * factor).astype(out[name].dtype)
    return out
```

```python
from contextlib import ExitStack

import concourse.bass as bass
from concourse import mybir

fp32 = mybir.dt.float32
i32 = mybir.dt.int32
ALU = mybir.AluOpType
ACT = mybir.ActivationFunctionType
AX = mybir.AxisListType

BATCH, SEQ = 64, 128
VOCAB, D = 8000, 256
HEADS = 16
HD = D // HEADS
STATE = 64
P = 128
C = D // P
PAIRS = BATCH // 2
STEPS = 8
HPS = 4
HPC = P // HD
VW = 32
EPS = 1e-5
SCALE = HD ** -0.5


def build(nc, x, emb, wqT, bq, wkT, bk, wvT, bv, woT, bo, b_w, c_wT, gate_wT, gate_b, log_decay, ffn_wT, out):
    ctx = ExitStack()
    with ctx:
        def sb(name, shape, dt=fp32):
            return ctx.enter_context(nc.sbuf_tensor(name, shape, dt))

        def bank(name):
            return ctx.enter_context(nc.psum_tensor(name, [P, 512], fp32))

        def sem(name):
            return ctx.enter_context(nc.semaphore(name))

        ident = sb("ident", [P, P])
        head_mask = sb("head_mask", [P, HPC])
        ones = sb("ones", [P, SEQ])
        neg_half = sb("neg_half", [P, 2])
        wq, wk, wv, wo, wg, wf = (sb(n, [P, C, D]) for n in ("wq", "wk", "wv", "wo", "wg", "wf"))
        wf_neg, wf_sign = sb("wf_neg", [P, C, D]), sb("wf_sign", [P, C, D])
        bw_sb, cw_sb = sb("bw_sb", [STATE, D]), sb("cw_sb", [STATE, D])
        w_state = sb("w_state", [P, C, D])
        bq_raw, bk_col, gb_raw, ld_col = (sb(n, [P, C]) for n in ("bq_raw", "bk_col", "gb_raw", "ld_col"))
        bq_col, gb_col = sb("bq_col", [P, C]), sb("gb_col", [P, C])
        e_ld, e_ld1, decay = sb("e_ld", [P, C]), sb("e_ld1", [P, C]), sb("decay", [P, C])
        powers = sb("powers", [P, C, SEQ])
        bv_row, bo_row = sb("bv_row", [P, D]), sb("bo_row", [P, D])
        x_raw = sb("x_raw", [BATCH, SEQ], i32)
        x_wrap, x_sum, x_clip = (sb(n, [BATCH, SEQ]) for n in ("x_wrap", "x_sum", "x_clip"))
        tok_ids = sb("tok_ids", [P, BATCH], i32)

        id_col = [[sb(f"id_col{p}{b}", [P, 1], i32) for b in range(2)] for p in range(2)]
        x_emb = [[sb(f"x_emb{p}{b}", [P, D]) for b in range(2)] for p in range(2)]
        xT = sb("xT", [P, C, 2, SEQ])
        kT = sb("kT", [P, C, 2, SEQ])
        qT = [sb(f"qT{p}", [P, C, 2, SEQ]) for p in range(2)]
        k_heads = [[sb(f"k_heads{p}{b}", [P, C, HPC, SEQ]) for b in range(2)] for p in range(2)]
        v_aug = [sb(f"v_aug{p}", [P, 2, HEADS, VW]) for p in range(2)]
        row_max = [sb(f"row_max{p}", [P, HPS]) for p in range(2)]
        probs = [sb(f"probs{p}", [P, HPS, SEQ]) for p in range(2)]
        probsT = [sb(f"probsT{p}", [P, HPS, SEQ]) for p in range(2)]
        ctx_raw = [sb(f"ctx_raw{b}", [P, 4, SEQ]) for b in range(2)]
        inv_sum = sb("inv_sum", [P, 2, HEADS])
        ctx_tok = sb("ctx_tok", [P, 2, D])
        ctxT = sb("ctxT", [P, C, 2, SEQ])
        h0, h1 = sb("h0", [P, 2, D]), sb("h1", [P, 2, D])
        stats1, stats2 = sb("stats1", [P, 2, 6]), sb("stats2", [P, 2, 6])
        mv1, mv2 = sb("mv1", [P, 2, 2]), sb("mv2", [P, 2, 2])
        ve1, ve2 = sb("ve1", [P, 2]), sb("ve2", [P, 2])
        rs1, rs2 = sb("rs1", [P, 2]), sb("rs2", [P, 2])
        xn1, xn2 = sb("xn1", [P, 2, D]), sb("xn2", [P, 2, D])
        xn1T, xn2T = sb("xn1T", [P, C, 2, SEQ]), sb("xn2T", [P, C, 2, SEQ])
        gate_tanh = sb("gate_tanh", [P, C, 2, SEQ])
        state_in = sb("state_in", [P, C, 2, SEQ])
        state = sb("state", [P, C, 2, SEQ])
        gated = sb("gated", [P, C, 2, SEQ])
        y = [sb(f"y{p}", [P, 2, D]) for p in range(2)]

        ps_s = [bank(f"ps_s{p}") for p in range(2)]
        ps_t = bank("ps_t")
        ps_c = bank("ps_c")
        g0, g1, g2, g3 = (bank(f"ps_g{i}") for i in range(4))

        w_loaded, small_loaded, x_loaded = sem("w_loaded"), sem("small_loaded"), sem("x_loaded")
        const_step, const_ready, ids_step, ids_fin = sem("const_step"), sem("const_ready"), sem("ids_step"), sem("ids_fin")
        ids_turned, ids_ready, wstate_mm, prep_step, prep_done = (sem("ids_turned"), sem("ids_ready"), sem("wstate_mm"),
                                                      sem("prep_step"), sem("prep_done"))
        exp_ld, act_prep = sem("exp_ld"), sem("act_prep")
        col_copied, keys_masked, rs1_done, rs2_done = sem("col_copied"), sem("keys_masked"), sem("rs1_done"), sem("rs2_done")
        gathered = [[sem(f"gathered{p}{b}") for b in range(2)] for p in range(2)]
        stored = [sem(f"stored{p}") for p in range(2)]
        pe_x, pe_k, pe_q, pe_v = sem("pe_x"), sem("pe_k"), sem("pe_q"), sem("pe_v")
        pe_scores, pe_pT, pe_pv = sem("pe_scores"), sem("pe_pT"), sem("pe_pv")
        pe_ctxrow, pe_ctxT, pe_o, pe_xn1T = sem("pe_ctxrow"), sem("pe_ctxT"), sem("pe_o"), sem("pe_xn1T")
        pe_gate, pe_state, pe_gated, pe_xn2T, pe_ffn = (sem("pe_gate"), sem("pe_state"), sem("pe_gated"),
                                                        sem("pe_xn2T"), sem("pe_ffn"))
        act_x, act_k, act_q, act_exp, act_pT, act_ctx = (sem("act_x"), sem("act_k"), sem("act_q"), sem("act_exp"),
                                                         sem("act_pT"), sem("act_ctx"))
        act_ctxT, act_xn1T, act_tanh, act_xn2T = sem("act_ctxT"), sem("act_xn1T"), sem("act_tanh"), sem("act_xn2T")
        dve_max, dve_sub, dve_v, dve_inv, dve_ctx = (sem("dve_max"), sem("dve_sub"), sem("dve_v"), sem("dve_inv"),
                                                     sem("dve_ctx"))
        dve_h0, dve_st1, dve_mv1, dve_ve1, dve_xn1 = (sem("dve_h0"), sem("dve_st1"), sem("dve_mv1"), sem("dve_ve1"),
                                                      sem("dve_xn1"))
        dve_h1, dve_st2, dve_mv2, dve_ve2, dve_xn2 = (sem("dve_h1"), sem("dve_st2"), sem("dve_mv2"), sem("dve_ve2"),
                                                      sem("dve_xn2"))
        dve_in, dve_scan, dve_gated, dve_y = sem("dve_in"), sem("dve_scan"), sem("dve_gated"), sem("dve_y")

        block = ctx.enter_context(nc.Block())

        def exists(pair):
            return not isinstance(pair, int) or 0 <= pair < PAIRS

        def await_event(eng, semaphore, per, pair, nth):
            if exists(pair):
                eng.wait_ge(semaphore, pair * per + nth)

        def await_dma(eng, semaphore, pair, par):
            if exists(pair):
                eng.wait_ge(semaphore, pair * 8 + (16 - 8 * par))

        def turns(eng, turn):
            for t in range(-2, 2):
                turn(t, t % 2)
            with eng.Fori(1, PAIRS // 2 - 1) as body:
                turn(body * 2, 0)
                turn(body * 2 + 1, 1)
            for t in range(PAIRS - 2, PAIRS + 2):
                turn(t, t % 2)

        def before(t, s, back):
            return (t, s - back) if s >= back else (t - 1, s - back + STEPS)

        @block.sync
        def _(sp):
            sp.dma_start(x_raw[:], x).then_inc(x_loaded, 16)
            for dst, src in ((wk, wkT), (wq, wqT), (wv, wvT), (wo, woT), (wg, gate_wT), (wf, ffn_wT)):
                sp.dma_start(dst[:], src.rearrange("(c p) o -> p c o", p=P)).then_inc(w_loaded, 16)
            sp.dma_start(bw_sb[:], b_w).then_inc(w_loaded, 16)
            sp.dma_start(cw_sb[:], c_wT).then_inc(w_loaded, 16)

            def store(t, par):
                pair = t - 2
                if exists(pair):
                    await_event(sp, dve_y, 1, pair, 1)
                    dst = out.rearrange("(n b) p d -> n p b d", b=2)[pair]
                    sp.dma_start(dst, y[par][:]).then_inc(stored[par], 16)

            turns(sp, store)
            for par in range(2):
                sp.wait_ge(stored[par], 16 * (PAIRS // 2))

        @block.gpsimd
        def _(pool):
            nc.gpsimd.memset(ident[:], 0.0).then_inc(const_step, 1)
            nc.gpsimd.memset(head_mask[:], 1.0).then_inc(const_step, 1)
            pool.wait_ge(const_step, 2)
            nc.gpsimd.affine_select(out=ident[:], in_=ident[:], compare_op=ALU.not_equal, fill=1.0, base=0,
                                    pattern=[[-1, P]], channel_multiplier=1).then_inc(const_ready, 1)
            nc.gpsimd.affine_select(out=head_mask[:], in_=head_mask[:], compare_op=ALU.is_ge, fill=0.0, base=0,
                                    pattern=[[-HD, HPC]], channel_multiplier=1).then_inc(const_step, 1)
            pool.wait_ge(const_step, 3)
            nc.gpsimd.affine_select(out=head_mask[:], in_=head_mask[:], compare_op=ALU.is_ge, fill=0.0, base=HD - 1,
                                    pattern=[[HD, HPC]], channel_multiplier=-1).then_inc(const_step, 1)
            nc.gpsimd.memset(neg_half[:], -0.5).then_inc(const_step, 1)
            pool.wait_ge(const_step, 5)
            pool.wait_ge(ids_ready, 1)

            def copy_ids(pair, par):
                if not exists(pair):
                    return
                for b in range(2):
                    await_dma(pool, gathered[par][b], pair - 2, par)
                    nc.gpsimd.tensor_copy(id_col[par][b][:],
                                          tok_ids[:, bass.ds(pair * 2 + b, 1)]).then_inc(col_copied, 1)
                await_event(pool, col_copied, 2, pair, 2)
                await_event(pool, pe_x, 1, pair - 2, 1)

            def gather(pair, par):
                if not exists(pair):
                    return
                for b in range(2):
                    nc.gpsimd.indirect_dma_start(
                        x_emb[par][b][:], None, emb,
                        bass.IndirectOffsetOnAxis(ap=id_col[par][b][:], axis=0)).then_inc(gathered[par][b], 16)

            def mask_keys(pair, par, b, chunks):
                if not exists(pair):
                    return
                await_event(pool, pe_scores, STEPS, pair - 2, 4 * b + 4)
                for c in chunks:
                    await_event(pool, act_k, C, pair, c + 1)
                    nc.gpsimd.tensor_tensor(
                        k_heads[par][b][:, c],
                        kT[:, c, b, :].unsqueeze(1).to_broadcast([P, HPC, SEQ]),
                        head_mask[:].unsqueeze(2).to_broadcast([P, HPC, SEQ]),
                        ALU.mult).then_inc(keys_masked, 1)

            def turn(t, par):
                copy_ids(t + 2, par)
                mask_keys(t + 1, 1 - par, 0, [0])
                gather(t + 2, par)
                mask_keys(t + 1, 1 - par, 0, [1])
                if exists(t - 2):
                    await_event(pool, dve_ve2, 1, t - 2, 1)
                    await_event(pool, dve_xn2, 2, t - 3, 2)
                    nc.gpsimd.tensor_tensor(rs2[:], ve2[:], neg_half[:], ALU.pow).then_inc(rs2_done, 1)
                mask_keys(t + 1, 1 - par, 1, [0, 1])
                if exists(t - 1):
                    await_event(pool, dve_ve1, 1, t - 1, 1)
                    await_event(pool, dve_xn1, 2, t - 2, 2)
                    nc.gpsimd.tensor_tensor(rs1[:], ve1[:], neg_half[:], ALU.pow).then_inc(rs1_done, 1)

            turns(pool, turn)

        @block.scalar
        def _(act):
            for n, (dst, src) in enumerate(((bq_raw, bq), (bk_col, bk), (gb_raw, gate_b), (ld_col, log_decay))):
                act.dma_start(dst[:], src).then_inc(small_loaded, 16)
            act.dma_start(bv_row[:], bv.partition_broadcast(P)).then_inc(small_loaded, 16)
            act.dma_start(bo_row[:], bo.partition_broadcast(P)).then_inc(small_loaded, 16)
            act.wait_ge(small_loaded, 96)
            nc.scalar.activation(e_ld[:], ld_col[:], ACT.Exp, scale=-1.0).then_inc(exp_ld, 1)
            nc.scalar.mul(bq_col[:], bq_raw[:], SCALE).then_inc(act_prep, 1)
            nc.scalar.mul(gb_col[:], gb_raw[:], 0.5).then_inc(act_prep, 1)
            act.wait_ge(act_prep, 2)

            def turn(t, par):
                def exponentials(s):
                    if exists(t):
                        await_event(act, dve_sub, STEPS, t, s + 1)
                        nc.scalar.activation(probs[s % 2][:], probs[s % 2][:], ACT.Exp).then_inc(act_exp, 1)

                def move_probsT(s):
                    pair, st = before(t, s, 1)
                    if exists(pair):
                        await_event(act, pe_pT, STEPS, pair, st + 1)
                        await_event(act, pe_pv, STEPS, *after_two(pair, st))
                        nc.scalar.copy(probsT[st % 2][:], ps_t[:]).then_inc(act_pT, 1)

                def after_two(pair, st):
                    p2, s2 = before(pair, st, 2)
                    return p2, s2 + 1

                def move_ctx(pair, b):
                    if exists(pair):
                        await_event(act, pe_pv, STEPS, pair, 4 * b + 4)
                        await_event(act, pe_ctxrow, 2, pair - 1, b + 1)
                        nc.scalar.copy(ctx_raw[b][:], ps_c[:]).then_inc(act_ctx, 1)

                def move_block(pair, dst, src, filled, freed, done):
                    if exists(pair):
                        await_event(act, filled, 1, pair, 1)
                        await_event(act, freed, 1, pair - 1, 1)
                        nc.scalar.copy(dst[:], src[:]).then_inc(done, 1)

                move_block(t + 1, xT, g0, pe_x, pe_v, act_x)
                exponentials(0)
                if exists(t + 1):
                    await_event(act, pe_k, 1, t + 1, 1)
                    await_event(act, keys_masked, 4, t, 4)
                    for c in range(C):
                        nc.scalar.activation(kT[:, c], g0[:, c * 256:c * 256 + 256], ACT.Identity,
                                             bias=bk_col[:, c:c + 1]).then_inc(act_k, 1)
                move_probsT(0)
                exponentials(1)
                if exists(t + 1):
                    await_event(act, pe_q, 1, t + 1, 1)
                    await_event(act, pe_scores, STEPS, t - 1, STEPS)
                    for c in range(C):
                        nc.scalar.activation(qT[1 - par][:, c], g1[:, c * 256:c * 256 + 256], ACT.Identity,
                                             bias=bq_col[:, c:c + 1], scale=SCALE).then_inc(act_q, 1)
                move_probsT(1)
                move_ctx(t - 1, 1)
                exponentials(2)
                move_probsT(2)
                exponentials(3)
                move_block(t - 1, ctxT, g2, pe_ctxT, pe_o, act_ctxT)
                move_probsT(3)
                move_block(t - 2, xn2T, g3, pe_xn2T, pe_ffn, act_xn2T)
                exponentials(4)
                move_probsT(4)
                exponentials(5)
                move_probsT(5)
                move_ctx(t, 0)
                move_block(t - 1, xn1T, g2, pe_xn1T, pe_state, act_xn1T)
                exponentials(6)
                move_probsT(6)
                if exists(t - 1):
                    await_event(act, pe_gate, 1, t - 1, 1)
                    await_event(act, dve_gated, 1, t - 2, 1)
                    for c in range(C):
                        nc.scalar.activation(gate_tanh[:, c], g3[:, c * 256:c * 256 + 256], ACT.Tanh,
                                             bias=gb_col[:, c:c + 1], scale=0.5).then_inc(act_tanh, 1)
                exponentials(7)
                move_probsT(7)

            turns(act, turn)

        @block.vector
        def _(dve):
            nc.vector.memset(ones[:], 1.0).then_inc(prep_step, 1)
            nc.vector.memset(powers[:, :, 0:1], 0.5).then_inc(prep_step, 1)
            nc.vector.memset(state[:, :, :, 0:1], 0.0).then_inc(prep_step, 1)
            for par in range(2):
                nc.vector.memset(v_aug[par][:], 0.0).then_inc(prep_step, 1)
            dve.wait_ge(prep_step, 5)
            for par in range(2):
                nc.vector.memset(v_aug[par][:, :, :, HD:HD + 1], 1.0).then_inc(prep_step, 1)
            dve.wait_ge(x_loaded, 16)
            nc.vector.tensor_scalar(x_wrap[:], x_raw[:], 0.0, float(VOCAB), ALU.is_lt, ALU.mult).then_inc(ids_step, 1)
            dve.wait_ge(ids_step, 1)
            nc.vector.tensor_tensor(x_sum[:], x_raw[:], x_wrap[:], ALU.add).then_inc(ids_step, 1)
            dve.wait_ge(ids_step, 2)
            nc.vector.tensor_scalar(x_clip[:], x_sum[:], 0.0, float(VOCAB - 1), ALU.max, ALU.min).then_inc(ids_fin, 1)
            dve.wait_ge(ids_turned, 1)
            nc.vector.tensor_copy(tok_ids[:], ps_s[0][:, 0:BATCH]).then_inc(ids_ready, 1)
            dve.wait_ge(w_loaded, 16 * 8)
            nc.vector.tensor_scalar(wf_neg[:], wf[:], 0.0, None, ALU.is_lt).then_inc(prep_step, 1)
            dve.wait_ge(prep_step, 8)
            nc.vector.scalar_tensor_tensor(wf_sign[:], wf[:], 0.0, wf_neg[:], ALU.is_gt,
                                           ALU.subtract).then_inc(prep_done, 1)
            dve.wait_ge(exp_ld, 1)
            nc.vector.tensor_scalar(e_ld1[:], e_ld[:], 1.0, None, ALU.add).then_inc(prep_step, 1)
            dve.wait_ge(prep_step, 9)
            nc.vector.reciprocal(decay[:], e_ld1[:]).then_inc(prep_step, 1)
            dve.wait_ge(prep_step, 10)
            for c in range(C):
                nc.vector.tensor_tensor_scan(powers[:, c, 1:SEQ], decay[:, c:c + 1].to_broadcast([P, SEQ - 1]),
                                             state[:, 0, 0, 0:1].to_broadcast([P, SEQ - 1]), powers[:, c, 0:1],
                                             ALU.mult, ALU.add).then_inc(prep_step, 1)
            dve.wait_ge(wstate_mm, 1)
            nc.vector.tensor_copy(w_state[:], g0[:]).then_inc(prep_done, 1)
            dve.wait_ge(prep_step, 12)
            dve.wait_ge(small_loaded, 96)

            def turn(t, par):
                def softmax_shift(s):
                    if exists(t):
                        sc = ps_s[s % 2][:].rearrange("p (h k) -> p h k", h=HPS)
                        await_event(dve, pe_scores, STEPS, t, s + 1)
                        nc.vector.tensor_reduce(row_max[s % 2][:], sc, axis=AX.X, op=ALU.max).then_inc(dve_max, 1)
                        await_event(dve, dve_max, STEPS, t, s + 1)
                        p2, s2 = before(t, s, 2)
                        await_event(dve, pe_pT, STEPS, p2, s2 + 1)
                        nc.vector.tensor_tensor(probs[s % 2][:], sc,
                                                row_max[s % 2][:].unsqueeze(2).to_broadcast([P, HPS, SEQ]),
                                                ALU.subtract).then_inc(dve_sub, 1)

                def norm_stats(pair, h, done_h, stats, done_st):
                    await_event(dve, done_h, 1, pair, 1)
                    for b in range(2):
                        nc.vector.bn_stats(stats[:, b], h[:, b]).then_inc(done_st, 1)

                def await_stats(pair, done_st, used):
                    await_event(dve, used, 2, pair - 1, 2)
                    await_event(dve, done_st, 2, pair, 2)

                def norm_moments(stats, mv, ve, done_mv, done_ve, pair):
                    for b in range(2):
                        nc.vector.bn_aggr(mv[:, b], stats[:, b]).then_inc(done_mv, 1)
                    await_event(dve, done_mv, 2, pair, 2)
                    nc.vector.tensor_scalar(ve[:], mv[:, :, 1], EPS, None, ALU.add).then_inc(done_ve, 1)

                def norm_apply(pair, h, mv, rs, xn, rs_done, freed, done):
                    await_event(dve, rs_done, 1, pair, 1)
                    await_event(dve, freed, 1, pair - 1, 1)
                    for b in range(2):
                        nc.vector.tensor_scalar(xn[:, b], h[:, b], mv[:, b, 0:1], rs[:, b:b + 1],
                                                ALU.subtract, ALU.mult).then_inc(done, 1)

                softmax_shift(0)
                if exists(t - 2):
                    for c in range(C):
                        for b in range(2):
                            await_event(dve, dve_in, 1, t - 2, 1)
                            nc.vector.tensor_tensor_scan(state[:, c, b, 1:SEQ], ones[:, 0:SEQ - 1],
                                                         state_in[:, c, b, 0:SEQ - 1], 0.0,
                                                         ALU.mult, ALU.add).then_inc(dve_scan, 1)
                    await_event(dve, dve_scan, 4, t - 2, 4)
                    await_event(dve, act_tanh, 2, t - 2, 2)
                    await_event(dve, pe_gated, 1, t - 3, 1)
                    nc.vector.scalar_tensor_tensor(gated[:], gate_tanh[:], 1.0, state[:], ALU.add,
                                                   ALU.mult).then_inc(dve_gated, 1)
                softmax_shift(1)
                softmax_shift(2)
                if exists(t - 1):
                    for b, rows in ((0, g3), (1, g0)):
                        r = rows[:].rearrange("p (h w) -> p h w", w=VW)
                        await_event(dve, pe_ctxrow, 2, t - 1, b + 1)
                        nc.vector.reciprocal(inv_sum[:, b], r[:, :, HD]).then_inc(dve_inv, 1)
                        await_event(dve, dve_inv, 2, t - 1, b + 1)
                        await_event(dve, pe_ctxT, 1, t - 2, 1)
                        nc.vector.tensor_tensor(ctx_tok[:, b].rearrange("p (h w) -> p h w", w=HD), r[:, :, 0:HD],
                                                inv_sum[:, b].unsqueeze(2).to_broadcast([P, HEADS, HD]),
                                                ALU.mult).then_inc(dve_ctx, 1)
                if exists(t - 2):
                    await_event(dve, pe_gated, 1, t - 2, 1)
                    nc.vector.tensor_tensor(h1[:].rearrange("p b d -> p (b d)"), g2[:],
                                            h0[:].rearrange("p b d -> p (b d)"), ALU.add).then_inc(dve_h1, 1)
                    norm_stats(t - 2, h1, dve_h1, stats2, dve_st2)
                if exists(t - 2):
                    await_stats(t - 2, dve_st2, dve_xn2)
                softmax_shift(3)
                if exists(t - 2):
                    norm_moments(stats2, mv2, ve2, dve_mv2, dve_ve2, t - 2)
                if exists(t + 1):
                    await_event(dve, pe_v, 1, t + 1, 1)
                    await_event(dve, pe_pv, STEPS, t - 1, STEPS)
                    nc.vector.tensor_tensor(
                        v_aug[1 - par][:, :, :, 0:HD],
                        g1[:].rearrange("p (b h w) -> p b h w", b=2, w=HD),
                        bv_row[:].rearrange("p (h w) -> p h w", w=HD).unsqueeze(1).to_broadcast([P, 2, HEADS, HD]),
                        ALU.add).then_inc(dve_v, 1)
                if exists(t - 2):
                    norm_apply(t - 2, h1, mv2, rs2, xn2, rs2_done, pe_xn2T, dve_xn2)
                softmax_shift(4)
                if exists(t - 1):
                    await_event(dve, pe_o, 1, t - 1, 1)
                    nc.vector.tensor_tensor(h0[:], g0[:].rearrange("p (b d) -> p b d", b=2),
                                            bo_row[:].unsqueeze(1).to_broadcast([P, 2, D]),
                                            ALU.add).then_inc(dve_h0, 1)
                    norm_stats(t - 1, h0, dve_h0, stats1, dve_st1)
                if exists(t - 1):
                    await_stats(t - 1, dve_st1, dve_xn1)
                softmax_shift(5)
                if exists(t - 1):
                    norm_moments(stats1, mv1, ve1, dve_mv1, dve_ve1, t - 1)
                if exists(t - 2):
                    await_event(dve, pe_ffn, 1, t - 2, 1)
                    await_dma(dve, stored[par], t - 4, par)
                    nc.vector.tensor_tensor(y[par][:].rearrange("p b d -> p (b d)"), g1[:],
                                            h1[:].rearrange("p b d -> p (b d)"), ALU.add).then_inc(dve_y, 1)
                if exists(t - 1):
                    norm_apply(t - 1, h0, mv1, rs1, xn1, rs1_done, pe_xn1T, dve_xn1)
                softmax_shift(6)
                softmax_shift(7)
                if exists(t - 1):
                    await_event(dve, pe_state, 1, t - 1, 1)
                    await_event(dve, dve_scan, 4, t - 2, 4)
                    nc.vector.tensor_tensor(state_in[:], g1[:].rearrange("p (c b k) -> p c b k", c=C, b=2),
                                            powers[:].unsqueeze(2).to_broadcast([P, C, 2, SEQ]),
                                            ALU.mult).then_inc(dve_in, 1)

            turns(dve, turn)

        @block.tensor
        def _(pe):
            def mm(dst, lhsT, rhs, first=True, last=True):
                return nc.tensor.matmul(dst, lhsT, rhs, start=first, stop=last)

            pe.wait_ge(const_ready, 1)
            pe.wait_ge(ids_fin, 1)
            nc.tensor.transpose(ps_s[0][:, 0:BATCH], x_clip[:], ident[0:BATCH, 0:BATCH]).then_inc(ids_turned, 1)
            pe.wait_ge(w_loaded, 16 * 8)
            for c in range(C):
                last = mm(g0[:, c * D:c * D + D], bw_sb[:, c * P:c * P + P], cw_sb[:])
            last.then_inc(wstate_mm, 1)
            pe.wait_ge(ids_ready, 1)
            pe.wait_ge(prep_done, 2)

            def feature_major(dst, weight, src, done):
                for c in range(C):
                    for k in range(C):
                        last = mm(dst[:, c * 256:c * 256 + 256], weight[:, k, c * P:c * P + P],
                                  src[:, k].rearrange("p b s -> p (b s)"), k == 0, k == C - 1)
                last.then_inc(done, 1)

            def token_major(dst, weight, src, done):
                for b in range(2):
                    for k in range(C):
                        last = mm(dst[:, b * D:b * D + D], src[:, k, b], weight[:, k], k == 0, k == C - 1)
                last.then_inc(done, 1)

            def to_features(dst, src, done):
                for c in range(C):
                    for b in range(2):
                        at = (2 * c + b) * SEQ
                        last = nc.tensor.transpose(dst[:, at:at + SEQ], src(b)[:, c * P:c * P + P], ident[:])
                last.then_inc(done, 1)

            def turn(t, par):
                def scores(s):
                    if not exists(t):
                        return
                    b, g = divmod(s, 4)
                    c, h = divmod(g * HPS, HPC)
                    if s == 0:
                        await_event(pe, act_q, C, t, C)
                    if g % 2 == 0:
                        await_event(pe, keys_masked, 4, t, 2 * b + c + 1)
                    p2, s2 = before(t, s, 2)
                    await_event(pe, dve_sub, STEPS, p2, s2 + 1)
                    mm(ps_s[s % 2][:], qT[par][:, c, b],
                       k_heads[par][b][:, c, h:h + HPS].rearrange("p h k -> p (h k)")).then_inc(pe_scores, 1)

                def turn_probs(s):
                    pair, st = before(t, s, 1)
                    if not exists(pair):
                        return
                    await_event(pe, act_exp, STEPS, pair, st + 1)
                    p1, s1 = before(pair, st, 1)
                    await_event(pe, act_pT, STEPS, p1, s1 + 1)
                    for j in range(HPS):
                        last = nc.tensor.transpose(ps_t[:, j * SEQ:j * SEQ + SEQ], probs[st % 2][:, j], ident[:])
                    last.then_inc(pe_pT, 1)

                def context(s):
                    pair, st = before(t, s, 2)
                    if not exists(pair):
                        return
                    vp = par if s >= 2 else 1 - par
                    b, g = divmod(st, 4)
                    await_event(pe, act_pT, STEPS, pair, st + 1)
                    if st == 0:
                        await_event(pe, dve_v, 1, pair, 1)
                        await_event(pe, act_ctx, 2, pair - 1, 2)
                    if st == 4:
                        await_event(pe, act_ctx, 2, pair, 1)
                    for j in range(HPS):
                        last = mm(ps_c[VW * j:VW * j + VW, g * SEQ:g * SEQ + SEQ],
                                  v_aug[vp][:, b, g * HPS + j], probsT[st % 2][:, j])
                    last.then_inc(pe_pv, 1)

                def context_rows(b, dst):
                    await_event(pe, act_ctx, 2, t - 1, b + 1)
                    for g in range(4):
                        last = nc.tensor.transpose(dst[:, g * P:g * P + P], ctx_raw[b][:, g], ident[:])
                    last.then_inc(pe_ctxrow, 1)

                scores(0)
                if exists(t + 1):
                    await_event(pe, act_x, 1, t + 1, 1)
                    feature_major(g0, wk, xT, pe_k)
                turn_probs(0)
                context(0)
                scores(1)
                if exists(t + 1):
                    if exists(t - 2):
                        await_event(pe, dve_in, 1, t - 2, 1)
                    else:
                        await_event(pe, dve_v, 1, t, 1)
                    feature_major(g1, wq, xT, pe_q)
                turn_probs(1)
                context(1)
                if exists(t - 2):
                    await_event(pe, dve_gated, 1, t - 2, 1)
                    await_event(pe, act_xn1T, 1, t - 2, 1)
                    for b in range(2):
                        for c in range(C):
                            at = (2 * b + c) * SEQ
                            last = nc.tensor.transpose(g2[:, at:at + SEQ], gated[:, c, b], ident[:])
                    last.then_inc(pe_gated, 1)
                scores(2)
                if exists(t - 1):
                    await_event(pe, act_tanh, 2, t - 2, 2)
                    context_rows(0, g3)
                    if exists(t + 1):
                        await_event(pe, act_k, C, t + 1, C)
                    context_rows(1, g0)
                turn_probs(2)
                context(2)
                if exists(t + 1):
                    await_event(pe, act_q, C, t + 1, C)
                    token_major(g1, wv, xT, pe_v)
                scores(3)
                if exists(t - 1):
                    await_event(pe, dve_ctx, 2, t - 1, 2)
                    await_event(pe, dve_h1, 1, t - 2, 1)
                    to_features(g2, lambda b: ctx_tok[:, b], pe_ctxT)
                turn_probs(3)
                context(3)
                if exists(t - 2):
                    await_event(pe, dve_xn2, 2, t - 2, 2)
                    await_event(pe, dve_ctx, 2, t - 1, 1)
                    to_features(g3, lambda b: xn2[:, b], pe_xn2T)
                scores(4)
                if exists(t - 1):
                    await_event(pe, act_ctxT, 1, t - 1, 1)
                    token_major(g0, wo, ctxT, pe_o)
                turn_probs(4)
                context(4)
                scores(5)
                if exists(t - 2):
                    await_event(pe, act_xn2T, 1, t - 2, 1)
                    await_event(pe, dve_v, 1, t + 1, 1)
                    token_major(g1, wf_sign, xn2T, pe_ffn)
                turn_probs(5)
                context(5)
                if exists(t - 1):
                    await_event(pe, dve_xn1, 2, t - 1, 2)
                    to_features(g2, lambda b: xn1[:, b], pe_xn1T)
                scores(6)
                turn_probs(6)
                context(6)
                if exists(t - 1):
                    await_event(pe, act_xn1T, 1, t - 1, 1)
                    await_event(pe, act_xn2T, 1, t - 2, 1)
                    feature_major(g3, wg, xn1T, pe_gate)
                scores(7)
                if exists(t - 1):
                    if exists(t - 2):
                        await_event(pe, dve_y, 1, t - 2, 1)
                    else:
                        await_event(pe, dve_v, 1, t + 1, 1)
                    feature_major(g1, w_state, xn1T, pe_state)
                turn_probs(7)
                context(7)
                if exists(t + 2):
                    for b in range(2):
                        await_dma(pe, gathered[par][b], t + 2, par)
                    if exists(t - 1):
                        await_event(pe, dve_h0, 1, t - 1, 1)
                    else:
                        await_event(pe, act_k, C, t + 1, C)
                    to_features(g0, lambda b: x_emb[par][b], pe_x)

            turns(pe, turn)


def kernel(x, L0_tok_emb, L0_tok_Wq, L0_tok_bq, L0_tok_Wk, L0_tok_bk, L0_tok_Wv, L0_tok_bv, L0_tok_Wo, L0_tok_bo,
           L0_attn_B_w, L0_attn_C_w, L0_attn_gate_w, L0_attn_gate_b, L0_attn_log_decay, L0_ffn_weight):
    import numpy as np
    import concourse.bacc as bacc
    from concourse.bass_utils import run_bass_kernel_spmd

    def turned(w):
        return np.ascontiguousarray(np.asarray(w).T)

    def column(b):
        return turned(np.asarray(b).reshape(C, P))

    arrays = {
        "x": x, "emb": L0_tok_emb,
        "wqT": turned(L0_tok_Wq), "bq": column(L0_tok_bq), "wkT": turned(L0_tok_Wk), "bk": column(L0_tok_bk),
        "wvT": turned(L0_tok_Wv), "bv": L0_tok_bv, "woT": turned(L0_tok_Wo), "bo": L0_tok_bo,
        "b_w": L0_attn_B_w, "c_wT": turned(L0_attn_C_w), "gate_wT": turned(L0_attn_gate_w),
        "gate_b": column(L0_attn_gate_b), "log_decay": column(L0_attn_log_decay), "ffn_wT": turned(L0_ffn_weight),
    }
    arrays = {f"in_{n}": np.ascontiguousarray(np.asarray(a)) for n, a in arrays.items()}
    nc = bacc.Bacc("TRN2", target_bir_lowering=False, num_devices=1)
    args = [nc.dram_tensor(n, a.shape, mybir.dt.from_np(a.dtype), kind="ExternalInput").ap() for n, a in arrays.items()]
    out = nc.dram_tensor("out_0", (BATCH, SEQ, D), fp32, kind="ExternalOutput").ap()
    build(nc, *args, out)
    result = run_bass_kernel_spmd(nc, [arrays], core_ids=[0])
    return result.results[0]["out_0"]
```

```python
from contextlib import ExitStack

import concourse.bass as bass
from concourse import mybir

fp32 = mybir.dt.float32
f32r = mybir.dt.float32r
i32 = mybir.dt.int32
ALU = mybir.AluOpType
ACT = mybir.ActivationFunctionType
AX = mybir.AxisListType

BATCH, SEQ = 64, 128
VOCAB, D = 8000, 256
HEADS = 16
HD = D // HEADS
STATE = 64
P = 128
C = D // P
PAIRS = BATCH // 2
STEPS = 8
HPS = 4
HPC = P // HD
VW = 32
EPS = 1e-5
SCALE = HD ** -0.5


def build(nc, x, emb, wqT, bq, wkT, bk, wvT, bv, woT, bo, b_w, c_wT, gate_wT, gate_b, log_decay, ffn_wT, out):
    ctx = ExitStack()
    with ctx:
        def sb(name, shape, dt=fp32):
            return ctx.enter_context(nc.sbuf_tensor(name, shape, dt))

        def bank(name):
            return ctx.enter_context(nc.psum_tensor(name, [P, 512], fp32))

        def sem(name):
            return ctx.enter_context(nc.semaphore(name))

        ident = sb("ident", [P, P])
        head_rows = sb("head_rows", [P, HPC])
        head_mask = sb("head_mask", [P, HPS])
        ones = sb("ones", [P, SEQ])
        neg_half = sb("neg_half", [P, 2])
        raw = [sb(f"raw{i}", [P, C, D]) for i in range(3)]
        wk, wq, wv, wg, wo, ws = ([sb(f"{n}{part}", [P, C, D], f32r) for part in "hl"] 
                                  for n in ("wk", "wq", "wv", "wg", "wo", "ws"))
        wf_sign = sb("wf_sign", [P, C, D], f32r)
        bw_sb, cw_sb = sb("bw_sb", [STATE, D]), sb("cw_sb", [STATE, D])
        bq_raw, bk_col, gb_raw, ld_col = (sb(n, [P, C]) for n in ("bq_raw", "bk_col", "gb_raw", "ld_col"))
        bq_col, gb_col = sb("bq_col", [P, C]), sb("gb_col", [P, C])
        e_ld, e_ld1, decay = sb("e_ld", [P, C]), sb("e_ld1", [P, C]), sb("decay", [P, C])
        powers = sb("powers", [P, C, SEQ])
        bv_row, bo_row = sb("bv_row", [P, D]), sb("bo_row", [P, D])
        x_raw = sb("x_raw", [BATCH, SEQ], i32)
        x_wrap, x_sum, x_clip = (sb(n, [BATCH, SEQ]) for n in ("x_wrap", "x_sum", "x_clip"))
        tok_ids = sb("tok_ids", [P, BATCH], i32)

        id_col = [[sb(f"id_col{p}{b}", [P, 1], i32) for b in range(2)] for p in range(2)]
        x_emb = [[sb(f"x_emb{p}{b}", [P, D]) for b in range(2)] for p in range(2)]
        xT, ctxT, xn1T, xn2T = ([sb(f"{n}{part}", [P, C, 2, SEQ], f32r) for part in "hl"] 
                                for n in ("xT", "ctxT", "xn1T", "xn2T"))
        kT, qT = sb("kT", [P, C, 2 * SEQ]), sb("qT", [P, C, 2 * SEQ])
        q_parts = [sb(f"q_parts{p}", [P, C, 2, 2 * SEQ], f32r) for p in range(2)]
        k_parts = sb("k_parts", [P, 2, C, 2, 2 * SEQ], f32r)
        k_heads = [sb(f"k_heads{p}", [P, 2, 2, C, 2, HPS, SEQ], f32r) for p in range(2)]
        v_aug = [sb(f"v_aug{p}", [P, 2, HEADS, VW]) for p in range(2)]
        neg_max = [sb(f"neg_max{p}", [P, HPS]) for p in range(2)]
        probs = [sb(f"probs{p}", [P, HPS, SEQ]) for p in range(2)]
        probsT = [sb(f"probsT{p}", [P, HPS, SEQ]) for p in range(2)]
        ctx_raw = [sb(f"ctx_raw{b}", [P, 4, SEQ]) for b in range(2)]
        inv_sum = sb("inv_sum", [P, 2, HEADS])
        ctx_tok = sb("ctx_tok", [P, 2, D])
        h0 = [sb(f"h0{p}", [P, 2, D]) for p in range(2)]
        h1 = sb("h1", [P, 2, D])
        stats1, stats2 = sb("stats1", [P, 2, 6]), sb("stats2", [P, 2, 6])
        mv1, mv2 = sb("mv1", [P, 2, 2]), sb("mv2", [P, 2, 2])
        ve1, ve2 = sb("ve1", [P, 2]), sb("ve2", [P, 2])
        rs1, rs2 = sb("rs1", [P, 2]), sb("rs2", [P, 2])
        xn1, xn2 = sb("xn1", [P, 2, D]), sb("xn2", [P, 2, D])
        gate_tanh = sb("gate_tanh", [P, C, 2, SEQ])
        state_in = sb("state_in", [P, C, 2, SEQ])
        state = sb("state", [P, C, 2, SEQ])
        gated = sb("gated", [P, C, 2, SEQ])
        y = [sb(f"y{p}", [P, 2, D]) for p in range(2)]

        ps_s = [bank(f"ps_s{p}") for p in range(2)]
        ps_t = bank("ps_t")
        ps_c = bank("ps_c")
        g0, g1, g2, g3 = (bank(f"ps_g{i}") for i in range(4))

        k_swapped = sem("k_swapped")
        raw_loaded = [sem(f"raw_loaded{i}") for i in range(3)]
        w_high, w_low = sem("w_high"), sem("w_low")
        w_loaded, small_loaded, x_loaded = sem("w_loaded"), sem("small_loaded"), sem("x_loaded")
        const_step, const_ready, ids_step, ids_fin = sem("const_step"), sem("const_ready"), sem("ids_step"), sem("ids_fin")
        ids_turned, ids_ready, wstate_mm, prep_step, prep_done = (sem("ids_turned"), sem("ids_ready"), sem("wstate_mm"),
                                                      sem("prep_step"), sem("prep_done"))
        exp_ld, act_prep = sem("exp_ld"), sem("act_prep")
        col_copied, keys_masked, rs1_done, rs2_done = sem("col_copied"), sem("keys_masked"), sem("rs1_done"), sem("rs2_done")
        gathered = [[sem(f"gathered{p}{b}") for b in range(2)] for p in range(2)]
        stored = [sem(f"stored{p}") for p in range(2)]
        pe_x, pe_k, pe_q, pe_v = sem("pe_x"), sem("pe_k"), sem("pe_q"), sem("pe_v")
        pe_scores, pe_pT, pe_pv = sem("pe_scores"), sem("pe_pT"), sem("pe_pv")
        pe_ctxrow, pe_ctxT, pe_o, pe_xn1T = sem("pe_ctxrow"), sem("pe_ctxT"), sem("pe_o"), sem("pe_xn1T")
        pe_gate, pe_state, pe_gated, pe_xn2T, pe_ffn = (sem("pe_gate"), sem("pe_state"), sem("pe_gated"),
                                                        sem("pe_xn2T"), sem("pe_ffn"))
        act_x, act_k, act_q, act_exp, act_pT, act_ctx = (sem("act_x"), sem("act_k"), sem("act_q"), sem("act_exp"),
                                                         sem("act_pT"), sem("act_ctx"))
        act_ctxT, act_xn1T, act_tanh, act_xn2T = sem("act_ctxT"), sem("act_xn1T"), sem("act_tanh"), sem("act_xn2T")
        dve_max, dve_v, dve_inv, dve_ctx = (sem("dve_max"), sem("dve_v"), sem("dve_inv"),
                                                     sem("dve_ctx"))
        dve_h0, dve_st1, dve_mv1, dve_ve1, dve_xn1 = (sem("dve_h0"), sem("dve_st1"), sem("dve_mv1"), sem("dve_ve1"),
                                                      sem("dve_xn1"))
        dve_h1, dve_st2, dve_mv2, dve_ve2, dve_xn2 = (sem("dve_h1"), sem("dve_st2"), sem("dve_mv2"), sem("dve_ve2"),
                                                      sem("dve_xn2"))
        act_khi, act_qhi = sem("act_khi"), sem("act_qhi")
        dve_ctxlo = sem("dve_ctxlo")
        dve_klo, dve_qlo, dve_xlo, dve_xn1lo, dve_xn2lo = (sem("dve_klo"), sem("dve_qlo"), sem("dve_xlo"),
                                                           sem("dve_xn1lo"), sem("dve_xn2lo"))
        dve_in, dve_scan, dve_gated, dve_y = sem("dve_in"), sem("dve_scan"), sem("dve_gated"), sem("dve_y")

        block = ctx.enter_context(nc.Block())

        def exists(pair):
            return not isinstance(pair, int) or 0 <= pair < PAIRS

        def await_event(eng, semaphore, per, pair, nth):
            if exists(pair):
                eng.wait_ge(semaphore, pair * per + nth)

        def await_dma(eng, semaphore, pair, par):
            if exists(pair):
                eng.wait_ge(semaphore, pair * 8 + (16 - 8 * par))

        def turns(eng, turn):
            for t in range(-2, 6):
                turn(t, t % 2)
            with eng.Fori(3, PAIRS // 2 - 1) as body:
                turn(body * 2, 0)
                turn(body * 2 + 1, 1)
            for t in range(PAIRS - 2, PAIRS + 4):
                turn(t, t % 2)

        def before(t, s, back):
            return (t, s - back) if s >= back else (t - 1, s - back + STEPS)

        @block.sync
        def _(sp):
            sp.dma_start(x_raw[:], x).then_inc(x_loaded, 16)
            chunked = [w.rearrange("(c p) o -> p c o", p=P) 
                       for w in (wkT, wqT, wvT, gate_wT, ffn_wT, woT)]
            for i in range(3):
                sp.dma_start(raw[i][:], chunked[i]).then_inc(raw_loaded[i], 16)
            sp.dma_start(bw_sb[:], b_w).then_inc(w_loaded, 16)
            sp.dma_start(cw_sb[:], c_wT).then_inc(w_loaded, 16)
            for i in range(3):
                sp.wait_ge(w_low, i + 1)
                sp.dma_start(raw[i][:], chunked[3 + i]).then_inc(raw_loaded[i], 16)

            def swap_keys(t):
                if exists(t + 1):
                    for e in range(2):
                        await_event(sp, dve_klo, 2, t + 1, e + 1)
                        await_event(sp, keys_masked, 16, t, 16)
                        own, other = slice(64 * e, 64 * e + 64), slice(64 - 64 * e, 128 - 64 * e)
                        sp.dma_start(k_parts[other, :, :, e].bitcast(fp32),
                                     k_parts[own, :, :, e].bitcast(fp32)).then_inc(k_swapped, 16)

            def turn(t, par):
                if exists(t - 4):
                    await_event(sp, dve_y, 1, t - 4, 1)
                    dst = out.rearrange("(n b) p d -> n p b d", b=2)[t - 4]
                    sp.dma_start(dst, y[par][:]).then_inc(stored[par], 16)
                swap_keys(t)

            turns(sp, turn)
            for par in range(2):
                sp.wait_ge(stored[par], 16 * (PAIRS // 2))

        @block.gpsimd
        def _(pool):
            nc.gpsimd.memset(ident[:], 0.0).then_inc(const_step, 1)
            nc.gpsimd.memset(head_rows[:], 1.0).then_inc(const_step, 1)
            pool.wait_ge(const_step, 2)
            nc.gpsimd.affine_select(out=ident[:], in_=ident[:], compare_op=ALU.not_equal, fill=1.0, base=0,
                                    pattern=[[-1, P]], channel_multiplier=1).then_inc(const_ready, 1)
            nc.gpsimd.affine_select(out=head_rows[:], in_=head_rows[:], compare_op=ALU.is_ge, fill=0.0, base=0,
                                    pattern=[[-HD, HPC]], channel_multiplier=1).then_inc(const_step, 1)
            pool.wait_ge(const_step, 3)
            nc.gpsimd.affine_select(out=head_rows[:], in_=head_rows[:], compare_op=ALU.is_ge, fill=0.0, base=HD - 1,
                                    pattern=[[HD, HPC]], channel_multiplier=-1).then_inc(const_step, 1)
            nc.gpsimd.memset(neg_half[:], -0.5).then_inc(const_step, 1)
            pool.wait_ge(const_step, 5)
            nc.gpsimd.tensor_tensor(head_mask[:], head_rows[:, 0:HPS], head_rows[:, HPS:HPC],
                                    ALU.add).then_inc(const_step, 1)
            pool.wait_ge(const_step, 6)
            pool.wait_ge(ids_ready, 1)

            def copy_ids(pair, par):
                if not exists(pair):
                    return
                for b in range(2):
                    await_dma(pool, gathered[par][b], pair - 2, par)
                    nc.gpsimd.tensor_copy(id_col[par][b][:],
                                          tok_ids[:, bass.ds(pair * 2 + b, 1)]).then_inc(col_copied, 1)
                await_event(pool, col_copied, 2, pair, 2)
                await_event(pool, pe_x, 1, pair - 2, 1)

            def gather(pair, par):
                if not exists(pair):
                    return
                for b in range(2):
                    nc.gpsimd.indirect_dma_start(
                        x_emb[par][b][:], None, emb,
                        bass.IndirectOffsetOnAxis(ap=id_col[par][b][:], axis=0)).then_inc(gathered[par][b], 16)

            def mask_keys(pair, par, b, e):
                if not exists(pair):
                    return
                if e == 0:
                    await_event(pool, k_swapped, 32, pair, 32)
                    await_event(pool, pe_scores, STEPS, pair - 2, 4 * b + 4)
                for h in range(HPS):
                    dst = k_heads[par][:, b, :, :, e, h]
                    src = k_parts[:, :, :, e, b * SEQ:b * SEQ + SEQ].bitcast(fp32)
                    if e == 0 and h == 0:
                        done = nc.gpsimd.tensor_tensor(
                            dst, src, head_mask[:, h:h + 1].unsqueeze(2).unsqueeze(3).to_broadcast([P, 2, C, SEQ]),
                            ALU.mult)
                    else:
                        done = nc.gpsimd.tensor_scalar(dst, src, head_mask[:, h:h + 1], 0.0, ALU.mult, ALU.add)
                    done.then_inc(keys_masked, 1)

            def turn(t, par):
                mask_keys(t, par, 1, 0)
                mask_keys(t, par, 1, 1)
                copy_ids(t + 2, par)
                if exists(t - 2):
                    await_event(pool, dve_ve1, 1, t - 2, 1)
                    await_event(pool, dve_xn1, 2, t - 3, 2)
                    nc.gpsimd.tensor_tensor(rs1[:], ve1[:], neg_half[:], ALU.pow).then_inc(rs1_done, 1)
                gather(t + 2, par)
                if exists(t - 3):
                    await_event(pool, dve_ve2, 1, t - 3, 1)
                    await_event(pool, dve_xn2, 2, t - 4, 2)
                    nc.gpsimd.tensor_tensor(rs2[:], ve2[:], neg_half[:], ALU.pow).then_inc(rs2_done, 1)
                mask_keys(t + 1, 1 - par, 0, 0)
                mask_keys(t + 1, 1 - par, 0, 1)

            turns(pool, turn)

        @block.scalar
        def _(act):
            for n, (dst, src) in enumerate(((bq_raw, bq), (bk_col, bk), (gb_raw, gate_b), (ld_col, log_decay))):
                act.dma_start(dst[:], src).then_inc(small_loaded, 16)
            act.dma_start(bv_row[:], bv.partition_broadcast(P)).then_inc(small_loaded, 16)
            act.dma_start(bo_row[:], bo.partition_broadcast(P)).then_inc(small_loaded, 16)
            act.wait_ge(small_loaded, 96)
            nc.scalar.activation(e_ld[:], ld_col[:], ACT.Exp, scale=-1.0).then_inc(exp_ld, 1)
            nc.scalar.mul(bq_col[:], bq_raw[:], SCALE).then_inc(act_prep, 1)
            nc.scalar.mul(gb_col[:], gb_raw[:], 0.5).then_inc(act_prep, 1)
            act.wait_ge(act_prep, 2)

            def high_part(dst, src):
                nc.scalar.copy(dst[:], src[:]).then_inc(w_high, 1)

            for i, w in enumerate((wk, wq, wv)):
                act.wait_ge(raw_loaded[i], 16)
                high_part(w[0], raw[i])
            act.wait_ge(raw_loaded[0], 32)
            high_part(wg[0], raw[0])
            act.wait_ge(raw_loaded[2], 32)
            high_part(wo[0], raw[2])
            act.wait_ge(wstate_mm, 1)
            high_part(ws[0], g3)

            def turn(t, par):
                def exponentials(s):
                    if exists(t):
                        await_event(act, dve_max, STEPS, t, s + 1)
                        p2, s2 = before(t, s, 2)
                        await_event(act, pe_pT, STEPS, p2, s2 + 1)
                        for j in range(HPS):
                            last = nc.scalar.activation(probs[s % 2][:, j], ps_s[s % 2][:, j * SEQ:j * SEQ + SEQ],
                                                        ACT.Exp, bias=neg_max[s % 2][:, j:j + 1])
                        last.then_inc(act_exp, 1)

                def move_probsT(s):
                    pair, st = before(t, s, 2)
                    if exists(pair):
                        await_event(act, pe_pT, STEPS, pair, st + 1)
                        await_event(act, pe_pv, STEPS, *after_two(pair, st))
                        nc.scalar.copy(probsT[st % 2][:], ps_t[:]).then_inc(act_pT, 1)

                def after_two(pair, st):
                    p2, s2 = before(pair, st, 2)
                    return p2, s2 + 1

                def move_ctx(pair, b):
                    if exists(pair):
                        await_event(act, pe_pv, STEPS, pair, 4 * b + 4)
                        await_event(act, pe_ctxrow, 2, pair - 1, b + 1)
                        nc.scalar.copy(ctx_raw[b][:], ps_c[:]).then_inc(act_ctx, 1)

                def move_block(pair, dst, src, filled, freed, done):
                    if exists(pair):
                        await_event(act, filled, 1, pair, 1)
                        await_event(act, freed, 1, pair - 1, 1)
                        nc.scalar.copy(dst[:], src[:]).then_inc(done, 1)

                move_probsT(0)
                exponentials(0)
                move_probsT(1)
                exponentials(1)
                move_probsT(2)
                move_block(t + 1, xT[0], g0, pe_x, pe_v, act_x)
                move_ctx(t - 1, 1)
                exponentials(2)
                move_probsT(3)
                exponentials(3)
                move_block(t - 2, xn1T[0], g3, pe_xn1T, pe_state, act_xn1T)
                move_probsT(4)
                if exists(t + 1):
                    await_event(act, pe_k, 1, t + 1, 1)
                    await_event(act, dve_klo, 2, t, 2)
                    for c in range(C):
                        nc.scalar.activation(kT[:, c], g1[:, c * 256:c * 256 + 256], ACT.Identity,
                                             bias=bk_col[:, c:c + 1]).then_inc(act_k, 1)
                    await_event(act, act_k, C, t + 1, C)
                    await_event(act, keys_masked, 16, t, 16)
                    for e in range(2):
                        own = slice(64 * e, 64 * e + 64)
                        nc.scalar.copy(k_parts[own, 0, :, e], kT[own]).then_inc(act_khi, 1)
                exponentials(4)
                move_probsT(5)
                if exists(t + 1):
                    await_event(act, pe_q, 1, t + 1, 1)
                    await_event(act, dve_qlo, 2, t, 2)
                    for c in range(C):
                        nc.scalar.activation(qT[:, c], g0[:, c * 256:c * 256 + 256], ACT.Identity,
                                             bias=bq_col[:, c:c + 1], scale=SCALE).then_inc(act_q, 1)
                    await_event(act, act_q, C, t + 1, C)
                    await_event(act, pe_scores, STEPS, t - 1, STEPS)
                    for e in range(2):
                        own = slice(64 * e, 64 * e + 64)
                        nc.scalar.copy(q_parts[1 - par][own, :, e], qT[own]).then_inc(act_qhi, 1)
                exponentials(5)
                move_probsT(6)
                move_block(t - 1, ctxT[0], g2, pe_ctxT, pe_o, act_ctxT)
                move_ctx(t, 0)
                exponentials(6)
                if exists(t - 2):
                    await_event(act, pe_gate, 1, t - 2, 1)
                    await_event(act, dve_gated, 1, t - 3, 1)
                    for c in range(C):
                        nc.scalar.activation(gate_tanh[:, c], g1[:, c * 256:c * 256 + 256], ACT.Tanh,
                                             bias=gb_col[:, c:c + 1], scale=0.5).then_inc(act_tanh, 1)
                move_probsT(7)
                move_block(t - 3, xn2T[0], g3, pe_xn2T, pe_ffn, act_xn2T)
                exponentials(7)

            turns(act, turn)

        @block.vector
        def _(dve):
            nc.vector.memset(ones[:], 1.0).then_inc(prep_step, 1)
            nc.vector.memset(powers[:, :, 0:1], 0.5).then_inc(prep_step, 1)
            nc.vector.memset(state[:, :, :, 0:1], 0.0).then_inc(prep_step, 1)
            for par in range(2):
                nc.vector.memset(v_aug[par][:], 0.0).then_inc(prep_step, 1)
            dve.wait_ge(prep_step, 5)
            for par in range(2):
                nc.vector.memset(v_aug[par][:, :, :, HD:HD + 1], 1.0).then_inc(prep_step, 1)
            dve.wait_ge(x_loaded, 16)
            nc.vector.tensor_scalar(x_wrap[:], x_raw[:], 0.0, float(VOCAB), ALU.is_lt, ALU.mult).then_inc(ids_step, 1)
            dve.wait_ge(ids_step, 1)
            nc.vector.tensor_tensor(x_sum[:], x_raw[:], x_wrap[:], ALU.add).then_inc(ids_step, 1)
            dve.wait_ge(ids_step, 2)
            nc.vector.tensor_scalar(x_clip[:], x_sum[:], 0.0, float(VOCAB - 1), ALU.max, ALU.min).then_inc(ids_fin, 1)
            dve.wait_ge(ids_turned, 1)
            nc.vector.tensor_copy(tok_ids[:], ps_s[0][:, 0:BATCH]).then_inc(ids_ready, 1)
            def low_part(part, src, n):
                dve.wait_ge(w_high, n)
                nc.vector.tensor_tensor(part[1][:], src, part[0][:].bitcast(fp32), ALU.subtract).then_inc(w_low, 1)

            for i, w in enumerate((wk, wq, wv)):
                low_part(w, raw[i][:], i + 1)
            low_part(wg, raw[0][:], 4)
            low_part(wo, raw[2][:], 5)
            low_part(ws, g3[:].rearrange("p (c o) -> p c o", c=C), 6)
            dve.wait_ge(raw_loaded[1], 32)
            dve.wait_ge(w_low, 4)
            nc.vector.tensor_scalar(raw[0][:], raw[1][:], 0.0, None, ALU.is_lt).then_inc(prep_step, 1)
            dve.wait_ge(prep_step, 8)
            nc.vector.scalar_tensor_tensor(wf_sign[:], raw[1][:], 0.0, raw[0][:], ALU.is_gt,
                                           ALU.subtract).then_inc(prep_done, 1)
            dve.wait_ge(exp_ld, 1)
            nc.vector.tensor_scalar(e_ld1[:], e_ld[:], 1.0, None, ALU.add).then_inc(prep_step, 1)
            dve.wait_ge(prep_step, 9)
            nc.vector.reciprocal(decay[:], e_ld1[:]).then_inc(prep_step, 1)
            dve.wait_ge(prep_step, 10)
            for c in range(C):
                nc.vector.tensor_tensor_scan(powers[:, c, 1:SEQ], decay[:, c:c + 1].to_broadcast([P, SEQ - 1]),
                                             state[:, 0, 0, 0:1].to_broadcast([P, SEQ - 1]), powers[:, c, 0:1],
                                             ALU.mult, ALU.add).then_inc(prep_step, 1)
            dve.wait_ge(prep_step, 12)
            dve.wait_ge(small_loaded, 96)

            def turn(t, par):
                def maxima(s):
                    if exists(t):
                        await_event(dve, pe_scores, STEPS, t, s + 1)
                        p2, s2 = before(t, s, 2)
                        await_event(dve, act_exp, STEPS, p2, s2 + 1)
                        nc.vector.tensor_reduce(neg_max[s % 2][:], ps_s[s % 2][:].rearrange("p (h k) -> p h k", h=HPS),
                                                axis=AX.X, op=ALU.max, negate=True).then_inc(dve_max, 1)

                def low_features(pair, parts, block, high_done, freed, done):
                    if exists(pair):
                        await_event(dve, high_done, 1, pair, 1)
                        await_event(dve, freed, 1, pair - 1, 1)
                        nc.vector.tensor_tensor(parts[1][:].rearrange("p c b s -> p (c b s)"), block[:],
                                                parts[0][:].rearrange("p c b s -> p (c b s)").bitcast(fp32),
                                                ALU.subtract).then_inc(done, 1)

                def norm_stats(pair, h, done_h, stats, done_st):
                    await_event(dve, done_h, 1, pair, 1)
                    for b in range(2):
                        nc.vector.bn_stats(stats[:, b], h[:, b]).then_inc(done_st, 1)

                def await_stats(pair, done_st, used):
                    await_event(dve, used, 2, pair - 1, 2)
                    await_event(dve, done_st, 2, pair, 2)

                def norm_moments(stats, mv, ve, done_mv, done_ve, pair):
                    for b in range(2):
                        nc.vector.bn_aggr(mv[:, b], stats[:, b]).then_inc(done_mv, 1)
                    await_event(dve, done_mv, 2, pair, 2)
                    nc.vector.tensor_scalar(ve[:], mv[:, :, 1], EPS, None, ALU.add).then_inc(done_ve, 1)

                def norm_apply(pair, h, mv, rs, xn, rs_done, freed, done):
                    await_event(dve, rs_done, 1, pair, 1)
                    await_event(dve, freed, 1, pair - 1, 1)
                    for b in range(2):
                        nc.vector.tensor_scalar(xn[:, b], h[:, b], mv[:, b, 0:1], rs[:, b:b + 1],
                                                ALU.subtract, ALU.mult).then_inc(done, 1)

                def context_norm(b, block):
                    if exists(t - 1):
                        r = block[:].rearrange("p (h w) -> p h w", w=VW)
                        await_event(dve, pe_ctxrow, 2, t - 1, b + 1)
                        nc.vector.reciprocal(inv_sum[:, b], r[:, :, HD]).then_inc(dve_inv, 1)
                        await_event(dve, dve_inv, 2, t - 1, b + 1)
                        await_event(dve, pe_ctxT, 1, t - 2, 1)
                        nc.vector.tensor_tensor(ctx_tok[:, b].rearrange("p (h w) -> p h w", w=HD), r[:, :, 0:HD],
                                                inv_sum[:, b].unsqueeze(2).to_broadcast([P, HEADS, HD]),
                                                ALU.mult).then_inc(dve_ctx, 1)

                maxima(0)
                if exists(t - 2):
                    await_event(dve, pe_o, 1, t - 2, 1)
                    nc.vector.tensor_tensor(h0[par][:], g2[:].rearrange("p (b d) -> p b d", b=2),
                                            bo_row[:].unsqueeze(1).to_broadcast([P, 2, D]),
                                            ALU.add).then_inc(dve_h0, 1)
                    norm_stats(t - 2, h0[par], dve_h0, stats1, dve_st1)
                if exists(t - 3):
                    for c in range(C):
                        for b in range(2):
                            await_event(dve, dve_in, 1, t - 3, 1)
                            nc.vector.tensor_tensor_scan(state[:, c, b, 1:SEQ], ones[:, 0:SEQ - 1],
                                                         state_in[:, c, b, 0:SEQ - 1], 0.0,
                                                         ALU.mult, ALU.add).then_inc(dve_scan, 1)
                    await_event(dve, dve_scan, 4, t - 3, 4)
                    await_event(dve, act_tanh, 2, t - 3, 2)
                    await_event(dve, pe_gated, 1, t - 4, 1)
                    nc.vector.scalar_tensor_tensor(gated[:], gate_tanh[:], 1.0, state[:], ALU.add,
                                                   ALU.mult).then_inc(dve_gated, 1)
                if exists(t - 4):
                    await_event(dve, pe_ffn, 1, t - 4, 1)
                    await_dma(dve, stored[par], t - 6, par)
                    nc.vector.tensor_tensor(y[par][:].rearrange("p b d -> p (b d)"), g0[:],
                                            h1[:].rearrange("p b d -> p (b d)"), ALU.add).then_inc(dve_y, 1)
                if exists(t - 2):
                    await_stats(t - 2, dve_st1, dve_xn1)
                maxima(1)
                if exists(t - 2):
                    norm_moments(stats1, mv1, ve1, dve_mv1, dve_ve1, t - 2)
                context_norm(0, g1)
                maxima(2)
                if exists(t):
                    await_event(dve, pe_v, 1, t, 1)
                    await_event(dve, pe_pv, STEPS, t - 2, STEPS)
                    nc.vector.tensor_tensor(
                        v_aug[par][:, :, :, 0:HD],
                        g2[:].rearrange("p (b h w) -> p b h w", b=2, w=HD),
                        bv_row[:].rearrange("p (h w) -> p h w", w=HD).unsqueeze(1).to_broadcast([P, 2, HEADS, HD]),
                        ALU.add).then_inc(dve_v, 1)
                low_features(t + 1, xT, g0, act_x, pe_v, dve_xlo)
                if exists(t - 2):
                    norm_apply(t - 2, h0[par], mv1, rs1, xn1, rs1_done, pe_xn1T, dve_xn1)
                if exists(t - 3):
                    await_event(dve, pe_gated, 1, t - 3, 1)
                    await_event(dve, dve_y, 1, t - 4, 1)
                    nc.vector.tensor_tensor(h1[:].rearrange("p b d -> p (b d)"), g3[:],
                                            h0[1 - par][:].rearrange("p b d -> p (b d)"), ALU.add).then_inc(dve_h1, 1)
                maxima(3)
                if exists(t - 3):
                    norm_stats(t - 3, h1, dve_h1, stats2, dve_st2)
                if exists(t - 3):
                    await_stats(t - 3, dve_st2, dve_xn2)
                maxima(4)
                if exists(t - 3):
                    norm_moments(stats2, mv2, ve2, dve_mv2, dve_ve2, t - 3)
                low_features(t - 2, xn1T, g3, act_xn1T, pe_state, dve_xn1lo)
                context_norm(1, g2)
                if exists(t + 1):
                    for e in range(2):
                        own = slice(64 * e, 64 * e + 64)
                        await_event(dve, act_khi, 2, t + 1, e + 1)
                        await_event(dve, k_swapped, 32, t, 32)
                        nc.vector.tensor_tensor(k_parts[own, 1, :, e], kT[own],
                                                k_parts[own, 0, :, e].bitcast(fp32),
                                                ALU.subtract).then_inc(dve_klo, 1)
                maxima(5)
                if exists(t - 3):
                    norm_apply(t - 3, h1, mv2, rs2, xn2, rs2_done, pe_xn2T, dve_xn2)
                if exists(t + 1):
                    for e in range(2):
                        own, other = slice(64 * e, 64 * e + 64), slice(64 - 64 * e, 128 - 64 * e)
                        await_event(dve, act_qhi, 2, t + 1, e + 1)
                        nc.vector.tensor_tensor(q_parts[1 - par][other, :, e], qT[own],
                                                q_parts[1 - par][own, :, e].bitcast(fp32),
                                                ALU.subtract).then_inc(dve_qlo, 1)
                maxima(6)
                low_features(t - 1, ctxT, g2, act_ctxT, pe_o, dve_ctxlo)
                maxima(7)
                if exists(t - 2):
                    await_event(dve, pe_state, 1, t - 2, 1)
                    await_event(dve, dve_scan, 4, t - 3, 4)
                    nc.vector.tensor_tensor(state_in[:], g0[:].rearrange("p (c b k) -> p c b k", c=C, b=2),
                                            powers[:].unsqueeze(2).to_broadcast([P, C, 2, SEQ]),
                                            ALU.mult).then_inc(dve_in, 1)
                low_features(t - 3, xn2T, g3, act_xn2T, pe_ffn, dve_xn2lo)

            turns(dve, turn)

        @block.tensor
        def _(pe):
            def mm(dst, lhsT, rhs, first=True, last=True):
                return nc.tensor.matmul(dst, lhsT, rhs, start=first, stop=last)

            pe.wait_ge(const_ready, 1)
            pe.wait_ge(ids_fin, 1)
            nc.tensor.transpose(ps_s[0][:, 0:BATCH], x_clip[:], ident[0:BATCH, 0:BATCH]).then_inc(ids_turned, 1)
            pe.wait_ge(w_loaded, 16 * 2)
            for c in range(C):
                last = mm(g3[:, c * D:c * D + D], bw_sb[:, c * P:c * P + P], cw_sb[:])
            last.then_inc(wstate_mm, 1)
            pe.wait_ge(ids_ready, 1)
            pe.wait_ge(w_low, 6)
            pe.wait_ge(prep_done, 1)

            PARTS = ((0, 0), (0, 1), (1, 0))

            def feature_major(dst, weight, src, done):
                for c in range(C):
                    terms = [(k, w, x) for k in range(C) for w, x in PARTS]
                    for n, (k, w, x) in enumerate(terms):
                        last = mm(dst[:, c * 256:c * 256 + 256], weight[w][:, k, c * P:c * P + P],
                                  src[x][:, k].rearrange("p b s -> p (b s)"), n == 0, n == len(terms) - 1)
                last.then_inc(done, 1)

            def token_major(dst, weight, src, parts, done):
                for b in range(2):
                    terms = [(k, w, x) for k in range(C) for w, x in parts]
                    for n, (k, w, x) in enumerate(terms):
                        last = mm(dst[:, b * D:b * D + D], src[x][:, k, b], weight[w][:, k],
                                  n == 0, n == len(terms) - 1)
                last.then_inc(done, 1)

            def to_features(dst, src, done):
                for c in range(C):
                    for b in range(2):
                        at = (2 * c + b) * SEQ
                        last = nc.tensor.transpose(dst[:, at:at + SEQ], src(b)[:, c * P:c * P + P], ident[:])
                last.then_inc(done, 1)

            def turn(t, par):
                def scores(s):
                    if not exists(t):
                        return
                    b, g = divmod(s, 4)
                    c, e = divmod(g, 2)
                    if s == 0:
                        await_event(pe, dve_qlo, 2, t, 2)
                    if g < 2:
                        await_event(pe, keys_masked, 16, t, 8 * b + 4 * g + 4)
                    for part in range(2):
                        last = mm(ps_s[s % 2][:], q_parts[par][:, c, e, b * SEQ:b * SEQ + SEQ],
                                  k_heads[par][:, b, part, c, e].rearrange("p h k -> p (h k)"), part == 0, part == 1)
                    last.then_inc(pe_scores, 1)

                def turn_probs(s):
                    pair, st = before(t, s, 2)
                    if not exists(pair):
                        return
                    await_event(pe, act_exp, STEPS, pair, st + 1)
                    p1, s1 = before(pair, st, 1)
                    await_event(pe, act_pT, STEPS, p1, s1 + 1)
                    for j in range(HPS):
                        last = nc.tensor.transpose(ps_t[:, j * SEQ:j * SEQ + SEQ], probs[st % 2][:, j], ident[:])
                    last.then_inc(pe_pT, 1)

                def context(s):
                    pair, st = before(t, s, 3)
                    if not exists(pair):
                        return
                    vp = par if s >= 3 else 1 - par
                    b, g = divmod(st, 4)
                    await_event(pe, act_pT, STEPS, pair, st + 1)
                    if st == 0:
                        await_event(pe, dve_v, 1, pair, 1)
                        await_event(pe, act_ctx, 2, pair - 1, 2)
                    if st == 4:
                        await_event(pe, act_ctx, 2, pair, 1)
                    for j in range(HPS):
                        last = mm(ps_c[VW * j:VW * j + VW, g * SEQ:g * SEQ + SEQ],
                                  v_aug[vp][:, b, g * HPS + j], probsT[st % 2][:, j])
                    last.then_inc(pe_pv, 1)

                def context_rows(b, dst):
                    await_event(pe, act_ctx, 2, t - 1, b + 1)
                    for g in range(4):
                        last = nc.tensor.transpose(dst[:, g * P:g * P + P], ctx_raw[b][:, g], ident[:])
                    last.then_inc(pe_ctxrow, 1)

                def await_first(*events):
                    for semaphore, per, pair, nth in events:
                        if exists(pair):
                            await_event(pe, semaphore, per, pair, nth)
                            return

                def attention(s):
                    turn_probs(s)
                    scores(s)
                    context(s)

                attention(0)
                if exists(t - 4):
                    await_event(pe, dve_xn2lo, 1, t - 4, 1)
                    await_first((dve_in, 1, t - 3, 1), (dve_y, 1, t - 5, 1))
                    token_major(g0, [wf_sign], xn2T, [(0, 0), (0, 1)], pe_ffn)
                if exists(t - 1):
                    await_first((act_tanh, 2, t - 3, 2), (act_k, C, t, C))
                    context_rows(0, g1)
                attention(1)
                if exists(t):
                    await_first((dve_h0, 1, t - 2, 1), (dve_v, 1, t - 1, 1))
                    token_major(g2, wv, xT, PARTS, pe_v)
                attention(2)
                if exists(t + 1):
                    for b in range(2):
                        await_dma(pe, gathered[1 - par][b], t + 1, 1 - par)
                    await_first((dve_y, 1, t - 4, 1), (dve_in, 1, t - 3, 1), (act_q, C, t, C))
                    to_features(g0, lambda b: x_emb[1 - par][b], pe_x)
                if exists(t - 3):
                    await_event(pe, dve_gated, 1, t - 3, 1)
                    for b in range(2):
                        for c in range(C):
                            at = (2 * b + c) * SEQ
                            last = nc.tensor.transpose(g3[:, at:at + SEQ], gated[:, c, b], ident[:])
                    last.then_inc(pe_gated, 1)
                attention(3)
                if exists(t - 1):
                    await_first((dve_v, 1, t, 1), (dve_h0, 1, t - 2, 1))
                    context_rows(1, g2)
                if exists(t + 1):
                    await_event(pe, dve_xlo, 1, t + 1, 1)
                    await_first((dve_ctx, 2, t - 1, 1), (act_k, C, t, C))
                    feature_major(g1, wk, xT, pe_k)
                if exists(t - 2):
                    await_event(pe, dve_xn1, 2, t - 2, 2)
                    await_event(pe, dve_h1, 1, t - 3, 1)
                    to_features(g3, lambda b: xn1[:, b], pe_xn1T)
                attention(4)
                if exists(t + 1):
                    feature_major(g0, wq, xT, pe_q)
                attention(5)
                if exists(t - 1):
                    await_event(pe, dve_ctx, 2, t - 1, 2)
                    to_features(g2, lambda b: ctx_tok[:, b], pe_ctxT)
                if exists(t - 2):
                    await_event(pe, dve_xn1lo, 1, t - 2, 1)
                    await_first((act_k, C, t + 1, C), (dve_ctx, 2, t - 1, 1), (act_tanh, 2, t - 3, 2))
                    feature_major(g1, wg, xn1T, pe_gate)
                attention(6)
                if exists(t - 2):
                    await_first((act_q, C, t + 1, C), (dve_y, 1, t - 4, 1))
                    feature_major(g0, ws, xn1T, pe_state)
                if exists(t - 3):
                    await_event(pe, dve_xn2, 2, t - 3, 2)
                    to_features(g3, lambda b: xn2[:, b], pe_xn2T)
                attention(7)
                if exists(t - 1):
                    await_event(pe, dve_ctxlo, 1, t - 1, 1)
                    token_major(g2, wo, ctxT, PARTS, pe_o)

            turns(pe, turn)


def kernel(x, L0_tok_emb, L0_tok_Wq, L0_tok_bq, L0_tok_Wk, L0_tok_bk, L0_tok_Wv, L0_tok_bv, L0_tok_Wo, L0_tok_bo,
           L0_attn_B_w, L0_attn_C_w, L0_attn_gate_w, L0_attn_gate_b, L0_attn_log_decay, L0_ffn_weight):
    import numpy as np
    import concourse.bacc as bacc
    from concourse.bass_utils import run_bass_kernel_spmd

    def turned(w):
        return np.ascontiguousarray(np.asarray(w).T)

    def column(b):
        return turned(np.asarray(b).reshape(C, P))

    arrays = {
        "x": x, "emb": L0_tok_emb,
        "wqT": turned(L0_tok_Wq), "bq": column(L0_tok_bq), "wkT": turned(L0_tok_Wk), "bk": column(L0_tok_bk),
        "wvT": turned(L0_tok_Wv), "bv": L0_tok_bv, "woT": turned(L0_tok_Wo), "bo": L0_tok_bo,
        "b_w": L0_attn_B_w, "c_wT": turned(L0_attn_C_w), "gate_wT": turned(L0_attn_gate_w),
        "gate_b": column(L0_attn_gate_b), "log_decay": column(L0_attn_log_decay), "ffn_wT": turned(L0_ffn_weight),
    }
    arrays = {f"in_{n}": np.ascontiguousarray(np.asarray(a)) for n, a in arrays.items()}
    nc = bacc.Bacc("TRN2", target_bir_lowering=False, num_devices=1)
    args = [nc.dram_tensor(n, a.shape, mybir.dt.from_np(a.dtype), kind="ExternalInput").ap() for n, a in arrays.items()]
    out = nc.dram_tensor("out_0", (BATCH, SEQ, D), fp32, kind="ExternalOutput").ap()
    build(nc, *args, out)
    result = run_bass_kernel_spmd(nc, [arrays], core_ids=[0])
    return result.results[0]["out_0"]
```
